# Optimizing a Trainium2 kernel written in Bass

```python
import numpy as np
import jax
import jax.numpy as jnp

def _softmax(x, axis=-1):
    return jax.nn.softmax(x, axis=axis)
def _gelu(x):
    return jax.nn.gelu(x, approximate=True)
def _silu(x):
    return jax.nn.silu(x)
def _sigmoid(x):
    return jax.nn.sigmoid(x)
def _layernorm(x, axis=-1, eps=1e-5):
    m = jnp.mean(x, axis=axis, keepdims=True)
    v = jnp.var(x, axis=axis, keepdims=True)
    return (x - m) / jnp.sqrt(v + eps)
def _scatter_add(tgt, idx, src, axis=0):
    return tgt.at[idx].add(src)
def _segment_sum(src, seg, n):
    return jax.ops.segment_sum(src, seg, n)

kernel_name = 'mk_conv_seq_d1_conv_nhwc512_499dba'

def setup_inputs(seed: int = 0):
    np.random.seed(seed)
    _w = jnp.asarray
    def _rec_inputs():
        import jax
        import jax.numpy as jnp
        _gk = jax.random.key(seed)
        x = -8.268e-05 + 0.9999 * jax.random.normal(jax.random.fold_in(_gk, 1), (32, 56, 56, 512), jnp.float32)
        return x
    x = _rec_inputs()
    def _L0_conv_setup():
        import jax, jax.numpy as jnp
        import numpy as np
        EPS = 0.001
        G = 8

        def bn(x, gamma, beta, mean, var):
            return gamma * (x - mean) * jax.lax.rsqrt(var + EPS) + beta

        def group_conv1x1(x, w, b):
            n, h, wd, c = x.shape
            g = w.shape[0]
            xg = x.reshape(n, h, wd, g, c // g)
            y = jnp.einsum('nhwgc,gcd->nhwgd', xg, w)
            return y.reshape(n, h, wd, -1) + b

        def channel_shuffle(x, g):
            n, h, w, c = x.shape
            return x.reshape(n, h, w, g, c // g).transpose(0, 1, 2, 4, 3).reshape(n, h, w, c)

        def depthwise3x3(x, w, b):
            c = x.shape[-1]
            y = jax.lax.conv_general_dilated(x, w, window_strides=(1, 1), padding='SAME', dimension_numbers=('NHWC', 'HWIO', 'NHWC'), feature_group_count=c)
            return y + b
        key = jax.random.key(seed)
        ks = jax.random.split(key, 4)
        N, H, W, C = (32, 56, 56, 512)
        B = C // 4
        d = {'x': jax.random.normal(ks[0], (N, H, W, C), jnp.float32), 'w1': jax.random.normal(ks[1], (G, C // G, B // G), jnp.float32) * 0.05, 'b1': jnp.zeros((B,), jnp.float32), 'dw_w': jax.random.normal(ks[2], (3, 3, 1, B), jnp.float32) * 0.05, 'dw_b': jnp.zeros((B,), jnp.float32), 'w2': jax.random.normal(ks[3], (G, B // G, C // G), jnp.float32) * 0.05, 'b2': jnp.zeros((C,), jnp.float32)}
        for i, ch in [(1, B), (2, B), (3, B), (4, C)]:
            d[f'bn{i}_g'] = jnp.ones((ch,), jnp.float32)
            d[f'bn{i}_b'] = jnp.zeros((ch,), jnp.float32)
            d[f'bn{i}_m'] = jnp.zeros((ch,), jnp.float32)
            d[f'bn{i}_v'] = jnp.ones((ch,), jnp.float32)
        return d
    _L0_conv_all = _L0_conv_setup()
    _L0_conv_in = {k: v for k, v in _L0_conv_all.items() if k in ('w1', 'b1', 'bn1_g', 'bn1_b', 'bn1_m', 'bn1_v', 'dw_w', 'dw_b', 'bn2_g', 'bn2_b', 'bn2_m', 'bn2_v', 'bn3_g', 'bn3_b', 'bn3_m', 'bn3_v', 'w2', 'b2', 'bn4_g', 'bn4_b', 'bn4_m', 'bn4_v', )}
    del _L0_conv_all

    return {
        "x": x,
        "L0_conv_w1": _L0_conv_in["w1"],
        "L0_conv_b1": _L0_conv_in["b1"],
        "L0_conv_bn1_g": _L0_conv_in["bn1_g"],
        "L0_conv_bn1_b": _L0_conv_in["bn1_b"],
        "L0_conv_bn1_m": _L0_conv_in["bn1_m"],
        "L0_conv_bn1_v": _L0_conv_in["bn1_v"],
        "L0_conv_dw_w": _L0_conv_in["dw_w"],
        "L0_conv_dw_b": _L0_conv_in["dw_b"],
        "L0_conv_bn2_g": _L0_conv_in["bn2_g"],
        "L0_conv_bn2_b": _L0_conv_in["bn2_b"],
        "L0_conv_bn2_m": _L0_conv_in["bn2_m"],
        "L0_conv_bn2_v": _L0_conv_in["bn2_v"],
        "L0_conv_bn3_g": _L0_conv_in["bn3_g"],
        "L0_conv_bn3_b": _L0_conv_in["bn3_b"],
        "L0_conv_bn3_m": _L0_conv_in["bn3_m"],
        "L0_conv_bn3_v": _L0_conv_in["bn3_v"],
        "L0_conv_w2": _L0_conv_in["w2"],
        "L0_conv_b2": _L0_conv_in["b2"],
        "L0_conv_bn4_g": _L0_conv_in["bn4_g"],
        "L0_conv_bn4_b": _L0_conv_in["bn4_b"],
        "L0_conv_bn4_m": _L0_conv_in["bn4_m"],
        "L0_conv_bn4_v": _L0_conv_in["bn4_v"],
    }

def reference(x, L0_conv_w1, L0_conv_b1, L0_conv_bn1_g, L0_conv_bn1_b, L0_conv_bn1_m, L0_conv_bn1_v, L0_conv_dw_w, L0_conv_dw_b, L0_conv_bn2_g, L0_conv_bn2_b, L0_conv_bn2_m, L0_conv_bn2_v, L0_conv_bn3_g, L0_conv_bn3_b, L0_conv_bn3_m, L0_conv_bn3_v, L0_conv_w2, L0_conv_b2, L0_conv_bn4_g, L0_conv_bn4_b, L0_conv_bn4_m, L0_conv_bn4_v):
    import jax
    import jax.numpy as jnp
    def _L0_conv_ref(x, w1, b1, bn1_g, bn1_b, bn1_m, bn1_v, dw_w, dw_b, bn2_g, bn2_b, bn2_m, bn2_v, bn3_g, bn3_b, bn3_m, bn3_v, w2, b2, bn4_g, bn4_b, bn4_m, bn4_v):
        import jax, jax.numpy as jnp
        import numpy as np
        EPS = 0.001
        G = 8

        def bn(x, gamma, beta, mean, var):
            return gamma * (x - mean) * jax.lax.rsqrt(var + EPS) + beta

        def group_conv1x1(x, w, b):
            n, h, wd, c = x.shape
            g = w.shape[0]
            xg = x.reshape(n, h, wd, g, c // g)
            y = jnp.einsum('nhwgc,gcd->nhwgd', xg, w)
            return y.reshape(n, h, wd, -1) + b

        def channel_shuffle(x, g):
            n, h, w, c = x.shape
            return x.reshape(n, h, w, g, c // g).transpose(0, 1, 2, 4, 3).reshape(n, h, w, c)

        def depthwise3x3(x, w, b):
            c = x.shape[-1]
            y = jax.lax.conv_general_dilated(x, w, window_strides=(1, 1), padding='SAME', dimension_numbers=('NHWC', 'HWIO', 'NHWC'), feature_group_count=c)
            return y + b
        h = group_conv1x1(x, w1, b1)
        h = jax.nn.relu(bn(h, bn1_g, bn1_b, bn1_m, bn1_v))
        h = channel_shuffle(h, G)
        h = bn(depthwise3x3(h, dw_w, dw_b), bn2_g, bn2_b, bn2_m, bn2_v)
        h = bn(h, bn3_g, bn3_b, bn3_m, bn3_v)
        h = bn(group_conv1x1(h, w2, b2), bn4_g, bn4_b, bn4_m, bn4_v)
        return jax.nn.relu(x + h)

    def _gn(v, G=32, eps=1e-5):
        B_, H_, W_, C_ = v.shape
        g = v.reshape(B_, H_, W_, G, C_ // G)
        m = jnp.mean(g, axis=(1, 2, 4), keepdims=True)
        s = jnp.var(g, axis=(1, 2, 4), keepdims=True)
        return ((g - m) / jnp.sqrt(s + eps)).reshape(v.shape)

    def _ln_c(v, eps=1e-6):
        m = jnp.mean(v, axis=-1, keepdims=True)
        s = jnp.var(v, axis=-1, keepdims=True)
        return (v - m) / jnp.sqrt(s + eps)

    def _ln_t(v, eps=1e-5):
        m = jnp.mean(v, axis=-1, keepdims=True)
        s = jnp.var(v, axis=-1, keepdims=True)
        return (v - m) / jnp.sqrt(s + eps)

    def _to_tokens(v):
        B_, H_, W_, C_ = v.shape
        return v.reshape(B_, H_ * W_, C_)
    def _from_tokens(t, like):
        return t.reshape(like.shape)

    x = _L0_conv_ref(x, L0_conv_w1, L0_conv_b1, L0_conv_bn1_g, L0_conv_bn1_b, L0_conv_bn1_m, L0_conv_bn1_v, L0_conv_dw_w, L0_conv_dw_b, L0_conv_bn2_g, L0_conv_bn2_b, L0_conv_bn2_m, L0_conv_bn2_v, L0_conv_bn3_g, L0_conv_bn3_b, L0_conv_bn3_m, L0_conv_bn3_v, L0_conv_w2, L0_conv_b2, L0_conv_bn4_g, L0_conv_bn4_b, L0_conv_bn4_m, L0_conv_bn4_v)
    return x


_drawn_inputs = setup_inputs


def setup_inputs(seed=0):
    import zlib

    import numpy as np

    out = dict(_drawn_inputs(seed))
    spreads = {'L0_conv_b1': (0.0, 0.8),
     'L0_conv_bn1_g': (1.0, 0.6),
     'L0_conv_bn1_b': (0.0, 0.8),
     'L0_conv_bn1_m': (0.0, 0.8),
     'L0_conv_bn1_v': (1.0, 0.6),
     'L0_conv_dw_b': (0.0, 0.373),
     'L0_conv_bn2_g': (1.0, 0.6),
     'L0_conv_bn2_b': (0.0, 0.349),
     'L0_conv_bn2_m': (0.0, 0.349),
     'L0_conv_bn2_v': (1.0, 0.6),
     'L0_conv_bn3_g': (1.0, 0.6),
     'L0_conv_bn3_b': (0.0, 0.461),
     'L0_conv_bn3_m': (0.0, 0.344),
     'L0_conv_bn3_v': (1.0, 0.6),
     'L0_conv_b2': (0.0, 0.1),
     'L0_conv_bn4_g': (1.0, 0.577),
     'L0_conv_bn4_b': (0.0, 0.1),
     'L0_conv_bn4_m': (0.0, 0.1),
     'L0_conv_bn4_v': (1.0, 0.6)}
    factors = {'L0_conv_w1': 6.776, 'L0_conv_dw_w': 5.215}
    for name, (base, spread) in spreads.items():
        noise = np.random.default_rng([zlib.crc32(name.encode()), seed]).standard_normal(out[name].shape)
        drawn = base * np.exp(spread * noise) if base else spread * noise
        out[name] = jnp.asarray(drawn.astype(out[name].dtype))
    for name, factor in factors.items():
        out[name] = (out[name] * factor).astype(out[name].dtype)
    return out
```

```python
import concourse.bass as bass
from concourse import mybir
from contextlib import ExitStack

FP32 = mybir.dt.float32
ALU = mybir.AluOpType
ACT = mybir.ActivationFunctionType

P = 128
N_IMG, H, W, C = 32, 56, 56, 512
GROUPS = 8
B = C // 4
KC = C // P
CIN, MID = C // GROUPS, B // GROUPS
EPS = 1e-3

TILES = 7
CHUNK = TILES * P
HALF_ROWS = CHUNK // W // 2
HALF = HALF_ROWS * W
HALVES_PER_IMAGE = H // HALF_ROWS
RING = 7
LOOPS = N_IMG * H * W // CHUNK // RING
LAG = 3
AHEAD = 3
T_BANKS, OUT_BANKS = 2, 3

PE_TAPS = [(-1, 0), (1, 0)]
DVE_TAPS = [(dr, dc) for dc in (-1, 1) for dr in (0, -1, 1)] + [(0, 0)]

TAP0 = 0
DW_B, G2, B2, M2, V2, G3, B3, M3, V3, C1_B, G1, B1, M1, V1 = range(9, 23)
N_PAR = 23
O_B, O_G4, O_B4, O_M4, O_V4 = range(5)


def tap_column(dr, dc):
    return TAP0 + 3 * (dr + 1) + dc + 1


def region(q, dr, dc):
    r0 = 1 if q == 0 and dr == -1 else 0
    r1 = HALF_ROWS - 1 if q == HALVES_PER_IMAGE - 1 and dr == 1 else HALF_ROWS
    return r0, r1, max(0, -dc), W - max(0, dc)


def build(nc, x, w1, w2, par_mid, par_out, out):
    x_c = x.rearrange("(t p) c -> p t c", p=P)
    out_c = out.rearrange("(t p) c -> p t c", p=P)
    ctx = ExitStack()
    with ctx:
        def sb(name, shape):
            return ctx.enter_context(nc.sbuf_tensor(name, shape, FP32))

        def pb(name):
            return ctx.enter_context(nc.psum_tensor(name, [P, 512], FP32))

        def sem(name):
            return ctx.enter_context(nc.semaphore(name))

        x_sb = sb("x_sb", [P, RING, TILES, C])
        xT = sb("xT", [P, KC, CHUNK])
        r_sb = sb("r_sb", [P, RING * CHUNK])
        s_sb = sb("s_sb", [P, RING * CHUNK])
        w1_sb = sb("w1_sb", [P, KC, 2 * MID])
        w2_sb = sb("w2_sb", [P, C])
        par = sb("par", [P, N_PAR])
        po = sb("po", [P, 5, C])
        bias_sb = sb("bias_sb", [P, C])
        ident = sb("ident", [P, P])
        diag = sb("diag", [P, len(PE_TAPS), P])
        beta_b = sb("beta_b", [P, P])
        tmp = sb("tmp", [P, 16])
        newton = sb("newton", [P, C])
        sq_in, sq_out = sb("sq_in", [P, 3 + C]), sb("sq_out", [P, 3 + C])

        t_ps = [pb(f"t_ps{i}") for i in range(T_BANKS)]
        o_ps = [pb(f"o_ps{i}") for i in range(OUT_BANKS)]
        c_ps = pb("c_ps")
        d_ps = [pb(f"d_ps{i}") for i in range(2)]

        loaded = [sem(f"loaded{i}") for i in range(RING)]
        stored = [sem(f"stored{i}") for i in range(RING)]
        params_in = sem("params_in")
        zeroed = sem("zeroed")
        ident_done = sem("ident_done")
        sqrt_in, sqrt_done = sem("sqrt_in"), sem("sqrt_done")
        prep = sem("prep")
        weights_ready = sem("weights_ready")
        beta_done = sem("beta_done")
        banks_written = sem("banks_written")
        setup_done = sem("setup_done")
        t_done = sem("t_done")
        xt_ready = sem("xt_ready")
        c1_done = sem("c1_done")
        r_ready = sem("r_ready")
        taps_done = sem("taps_done")
        dchain = sem("dchain")
        s_ready = sem("s_ready")
        seeded = sem("seeded")
        c2_done = sem("c2_done")
        out_ready = sem("out_ready")

        block = ctx.enter_context(nc.Block())

        def wait(eng, s, count):
            if not (isinstance(count, int) and count <= 0):
                eng.wait_ge(s, count)

        def out_bank(i, t):
            return (TILES * (i % RING) + t) % OUT_BANKS

        def before_in_bank(i, t):
            return next(d for d in range(1, 2 * OUT_BANKS)
                        if out_bank(i + (t - d) // TILES, (t - d) % TILES) == out_bank(i, t))

        def steps(eng, step):
            for i in range(RING):
                step(0, i)
            with eng.Fori(1, LOOPS) as loop:
                for i in range(RING):
                    step(loop, i)
            for i in range(LAG):
                step(LOOPS, i)

        def chunk_exists(loop, i, lag):
            return not isinstance(loop, int) or 0 <= RING * loop + i - lag < RING * LOOPS

        @block.sync
        def _(sp):
            sp.dma_start(par[:, :], par_mid).then_inc(params_in, 16)
            for k in range(5):
                sp.dma_start(po[:, k, :], par_out[k:k + 1, :].broadcast_to([P, C])).then_inc(params_in, 16)
            sp.wait_ge(zeroed, 2)
            w1_g = w1.rearrange("(k e) c m -> e c k m", e=2)
            for e in range(2):
                sp.dma_start(w1_sb[e * CIN:(e + 1) * CIN, :, e * MID:(e + 1) * MID], w1_g[e]).then_inc(params_in, 16)
            for j in range(MID):
                sp.dma_start(w2_sb[j:j + MID * (GROUPS - 1) + 1:MID, CIN * (j // 2):CIN * (j // 2 + 1)],
                             w2[j // 2, GROUPS * (j % 2):GROUPS * (j % 2 + 1), :]).then_inc(params_in, 16)

            def load(loop, i):
                g = loop * RING + i
                sp.dma_start(x_sb[:, i % RING], x_c[:, bass.ds(g * TILES, TILES), :]).then_inc(loaded[i % RING], 16)

            for i in range(RING - 1):
                load(0, i)

            def step(loop, i):
                if chunk_exists(loop, i, LAG):
                    g = loop * RING + i - LAG
                    sp.wait_ge(out_ready, (g + 1) * TILES)
                    slot = (i - LAG) % RING
                    sp.dma_start(out_c[:, bass.ds(g * TILES, TILES), :], x_sb[:, slot]).then_inc(stored[slot], 16)
                if chunk_exists(loop, i, -AHEAD) and not (isinstance(loop, int) and RING * loop + i + AHEAD < RING - 1):
                    ahead = i + AHEAD
                    slot = ahead % RING
                    g = loop * RING + ahead
                    wait(sp, stored[slot], 16 * (loop + ahead // RING))
                    sp.dma_start(x_sb[:, slot], x_c[:, bass.ds(g * TILES, TILES), :]).then_inc(loaded[slot], 16)

            for i in range(RING):
                step(0, i)
            with sp.Fori(1, LOOPS - 1) as loop:
                for i in range(RING):
                    step(loop, i)
            for i in range(RING + LAG):
                step(LOOPS - 1 + i // RING, i % RING)
            for slot in range(RING):
                sp.wait_ge(stored[slot], 16 * LOOPS)

        @block.gpsimd
        def _(pool):
            pool.memset(w1_sb[:, :, :], 0.0).then_inc(zeroed, 1)
            pool.memset(w2_sb[:, :], 0.0).then_inc(zeroed, 1)
            pool.memset(ident[:, :], 0.0).then_inc(ident_done, 1)
            pool.wait_ge(ident_done, 1)
            pool.affine_select(out=ident[:, :], in_=ident[:, :], compare_op=ALU.not_equal, fill=1.0, base=0,
                               pattern=[[-1, P]], channel_multiplier=1).then_inc(ident_done, 1)

        @block.scalar
        def _(act):
            act.wait_ge(sqrt_in, 1)
            nc.scalar.activation(sq_out[:, :], sq_in[:, :], ACT.Sqrt).then_inc(sqrt_done, 1)
            act.wait_ge(setup_done, 1)

            def copy_xt(loop, i, t):
                act.wait_ge(t_done, (loop * RING + i) * TILES + t + 1)
                nc.scalar.copy(xT[:, :, t * P:(t + 1) * P],
                               t_ps[t % T_BANKS][:, :].rearrange("p (k m) -> p k m", k=KC)).then_inc(xt_ready, 1)

            def relu_r(loop, i, e):
                n = (loop * RING + i) * 2 + e
                act.wait_ge(c1_done, n + 1)
                at = ((2 * i + e) % (2 * RING)) * HALF
                nc.scalar.activation(r_sb[:, at:at + HALF], c_ps[:, 0:HALF], ACT.Relu, bias=tmp[:, 15:16],
                                     scale=tmp[:, 14:15]).then_inc(r_ready, 1)

            def relu_out(loop, i, t):
                act.wait_ge(c2_done, (loop * RING + i) * TILES + t + 1)
                nc.scalar.activation(x_sb[:, i % RING, t], o_ps[out_bank(i, t)][:, :], ACT.Relu).then_inc(out_ready, 1)

            def step(loop, i):
                for t in range(TILES):
                    if chunk_exists(loop, i, 0):
                        copy_xt(loop, i, t)
                    if chunk_exists(loop, i, LAG):
                        relu_out(loop, i - LAG, t)
                    if t == 0 and chunk_exists(loop, i, 1):
                        relu_r(loop, i - 1, 1)
                    if t == 4 and chunk_exists(loop, i, 0):
                        relu_r(loop, i, 0)

            steps(act, step)

        @block.vector
        def _(dve):
            count = [0]

            def then(ins):
                count[0] += 1
                ins.then_inc(prep, 1)
                dve.wait_ge(prep, count[0])

            def col(c):
                return par[:, c:c + 1]

            def tcol(c):
                return tmp[:, c:c + 1]

            dve.wait_ge(params_in, 16 * (1 + 5 + 2 + MID))
            for k, v in enumerate((V1, V2, V3)):
                then(nc.vector.tensor_scalar(sq_in[:, k:k + 1], col(v), EPS, None, ALU.add))
            nc.vector.tensor_scalar(sq_in[:, 3:3 + C], po[:, O_V4, :], EPS, None, ALU.add).then_inc(sqrt_in, 1)
            dve.wait_ge(sqrt_done, 1)
            then(nc.vector.reciprocal(sq_out[:, :], sq_out[:, :]))
            full = [(sq_in[:, 0:3], sq_out[:, 0:3], newton[:, 0:3]), (sq_in[:, 3:3 + C], sq_out[:, 3:3 + C], newton[:, :])]
            for _ in range(2):
                for v, y, n in full:
                    then(nc.vector.tensor_tensor(n, y, y, ALU.mult))
                    then(nc.vector.tensor_tensor(n, n, v, ALU.mult))
                    then(nc.vector.tensor_scalar(n, n, -0.5, 1.5, ALU.mult, ALU.add))
                    then(nc.vector.tensor_tensor(y, y, n, ALU.mult))
            inv1, inv2, inv3, inv4 = sq_out[:, 0:1], sq_out[:, 1:2], sq_out[:, 2:3], sq_out[:, 3:3 + C]
            then(nc.vector.tensor_tensor(tcol(14), col(G1), inv1, ALU.mult))
            then(nc.vector.tensor_tensor(tcol(0), col(C1_B), col(M1), ALU.subtract))
            then(nc.vector.scalar_tensor_tensor(tcol(15), tcol(0), tcol(14), col(B1), ALU.mult, ALU.add))
            then(nc.vector.tensor_tensor(tcol(1), col(G2), inv2, ALU.mult))
            then(nc.vector.tensor_tensor(tcol(2), col(G3), inv3, ALU.mult))
            then(nc.vector.tensor_tensor(tcol(3), tcol(1), tcol(2), ALU.mult))
            then(nc.vector.tensor_tensor(tcol(4), col(DW_B), col(M2), ALU.subtract))
            then(nc.vector.scalar_tensor_tensor(tcol(5), tcol(4), tcol(1), col(B2), ALU.mult, ALU.add))
            then(nc.vector.tensor_tensor(tcol(6), tcol(5), col(M3), ALU.subtract))
            then(nc.vector.scalar_tensor_tensor(tcol(7), tcol(6), tcol(2), col(B3), ALU.mult, ALU.add))
            then(nc.vector.tensor_scalar(par[:, TAP0:TAP0 + 9], par[:, TAP0:TAP0 + 9], tcol(3), None, ALU.mult))
            then(nc.vector.tensor_tensor(newton[:, :], po[:, O_G4, :], inv4, ALU.mult))
            then(nc.vector.tensor_tensor(w2_sb[:, :], w2_sb[:, :], newton[:, :], ALU.mult))
            then(nc.vector.tensor_tensor(bias_sb[:, :], po[:, O_B, :], po[:, O_M4, :], ALU.subtract))
            then(nc.vector.tensor_tensor(bias_sb[:, :], bias_sb[:, :], newton[:, :], ALU.mult))
            then(nc.vector.tensor_tensor(bias_sb[:, :], bias_sb[:, :], po[:, O_B4, :], ALU.add))
            dve.wait_ge(ident_done, 2)
            for k, (dr, dc) in enumerate(PE_TAPS):
                then(nc.vector.tensor_scalar(diag[:, k], ident[:, :], col(tap_column(dr, dc)), None, ALU.mult))
            then(nc.vector.memset(beta_b[:, :], 1.0))
            nc.vector.tensor_scalar(beta_b[:, :], beta_b[:, :], tcol(7), None, ALU.mult).then_inc(weights_ready, 1)
            dve.wait_ge(banks_written, OUT_BANKS)
            nc.vector.tensor_tensor(bias_sb[:, :], bias_sb[:, :], o_ps[0][:, :], ALU.add).then_inc(setup_done, 1)
            dve.wait_ge(setup_done, 1)

            def seed(loop, i, t):
                before = (loop * RING + i) * TILES + t - before_in_bank(i, t)
                wait(dve, out_ready, before + 1)
                nc.vector.tensor_tensor(o_ps[out_bank(i, t)][:, :], x_sb[:, i % RING, t], bias_sb[:, :],
                                        ALU.add).then_inc(seeded, 1)

            def tap(loop, h, k):
                q = h % HALVES_PER_IMAGE
                n = loop * 2 * RING + h
                base = (h % (2 * RING)) * HALF
                dr, dc = DVE_TAPS[k]
                r0, r1, c0, c1 = region(q, dr, dc)
                if k == 0:
                    dve.wait_ge(taps_done, n + 1)
                else:
                    dve.wait_ge(dchain, (len(DVE_TAPS) - 1) * n + k)
                acc = d_ps[h % 2][:, 0:HALF].rearrange("p (r c) -> p r c", c=W)[:, r0:r1, c0:c1]
                at = base + (r0 + dr) * W
                src = r_sb[:, at:at + (r1 - r0) * W].rearrange("p (r c) -> p r c", c=W)[:, :, c0 + dc:c1 + dc]
                weight = par[:, tap_column(dr, dc):tap_column(dr, dc) + 1]
                if k < len(DVE_TAPS) - 1:
                    nc.vector.scalar_tensor_tensor(acc, src, weight, acc, ALU.mult, ALU.add).then_inc(dchain, 1)
                else:
                    s3 = s_sb[:, base:base + HALF].rearrange("p (r c) -> p r c", c=W)
                    nc.vector.scalar_tensor_tensor(s3, src, weight, acc, ALU.mult, ALU.add).then_inc(s_ready, 1)

            def step(loop, i):
                work = [(h, k) for h, lag in ((2 * i - 3, 2), (2 * i - 2, 1)) if chunk_exists(loop, i, lag)
                        for k in range(len(DVE_TAPS))]
                for t in range(TILES):
                    if chunk_exists(loop, i, LAG):
                        seed(loop, i - LAG, t)
                    for h, k in work[2 * t:2 * t + 2]:
                        tap(loop, h, k)
                assert len(work) <= 2 * TILES

            steps(dve, step)

        @block.tensor
        def _(pe):
            pe.wait_ge(weights_ready, 1)
            for k in range(OUT_BANKS):
                nc.tensor.matmul(o_ps[k][:, :], beta_b[:, :], w2_sb[:, :], start=True, stop=True).then_inc(banks_written, 1)
            pe.wait_ge(setup_done, 1)

            def transpose_tile(loop, i, t):
                if t == 0:
                    pe.wait_ge(loaded[i % RING], 16 * (loop + 1))
                n = (loop * RING + i) * TILES + t
                wait(pe, xt_ready, n - (T_BANKS - 1) if t else n)
                for k in range(KC):
                    last = nc.tensor.transpose(t_ps[t % T_BANKS][:, k * P:(k + 1) * P],
                                               x_sb[:, i % RING, t, k * P:(k + 1) * P], ident[:, :])
                last.then_inc(t_done, 1)

            def conv1(loop, i, e):
                n = (loop * RING + i) * 2 + e
                pe.wait_ge(xt_ready, (loop * RING + i) * TILES + (TILES if e else TILES // 2 + 1))
                wait(pe, r_ready, n)
                for k in range(KC):
                    last = nc.tensor.matmul(c_ps[2 * MID * k:2 * MID * (k + 1), 0:HALF], w1_sb[:, k],
                                            xT[:, k, e * HALF:(e + 1) * HALF], start=True, stop=True)
                last.then_inc(c1_done, 1)

            def pe_taps(loop, h):
                q = h % HALVES_PER_IMAGE
                n = loop * 2 * RING + h
                base = (h % (2 * RING)) * HALF
                wait(pe, s_ready, n - 1)
                pe.wait_ge(r_ready, n + (1 if q == HALVES_PER_IMAGE - 1 else 2))
                order = PE_TAPS if q else PE_TAPS[::-1]
                for m, (dr, dc) in enumerate(order):
                    r0, r1, _, _ = region(q, dr, dc)
                    last = nc.tensor.matmul(d_ps[h % 2][:, r0 * W:r1 * W], diag[:, PE_TAPS.index((dr, dc))],
                                            r_sb[:, base + (r0 + dr) * W:base + (r1 + dr) * W],
                                            start=m == 0, stop=m == len(order) - 1)
                last.then_inc(taps_done, 1)

            def conv2(loop, i, t):
                n = loop * RING + i
                pe.wait_ge(s_ready, n * 2 + (1 if (t + 1) * P <= HALF else 2))
                pe.wait_ge(seeded, n * TILES + t + 1)
                at = (i % RING) * CHUNK + t * P
                nc.tensor.matmul(o_ps[out_bank(i, t)][:, :], s_sb[:, at:at + P], w2_sb[:, :], start=False, stop=True,
                                 skip_group_check=True).then_inc(c2_done, 1)

            def step(loop, i):
                for t in range(TILES):
                    if chunk_exists(loop, i, 0):
                        transpose_tile(loop, i, t)
                    if chunk_exists(loop, i, LAG):
                        conv2(loop, i - LAG, t)
                    if t == 0 and chunk_exists(loop, i, 1):
                        conv1(loop, i - 1, 1)
                    if t == 1 and chunk_exists(loop, i, 1):
                        pe_taps(loop, 2 * i - 2)
                    if t == 4 and chunk_exists(loop, i, 0):
                        conv1(loop, i, 0)
                    if t == 6 and chunk_exists(loop, i, 1):
                        pe_taps(loop, 2 * i - 1)

            steps(pe, step)


INPUTS = ["x", "L0_conv_w1", "L0_conv_w2", "par_mid", "par_out"]


def kernel(x, L0_conv_w1, L0_conv_b1, L0_conv_bn1_g, L0_conv_bn1_b, L0_conv_bn1_m, L0_conv_bn1_v, L0_conv_dw_w,
           L0_conv_dw_b, L0_conv_bn2_g, L0_conv_bn2_b, L0_conv_bn2_m, L0_conv_bn2_v, L0_conv_bn3_g, L0_conv_bn3_b,
           L0_conv_bn3_m, L0_conv_bn3_v, L0_conv_w2, L0_conv_b2, L0_conv_bn4_g, L0_conv_bn4_b, L0_conv_bn4_m,
           L0_conv_bn4_v):
    import numpy as np
    from concourse import bacc
    from concourse.bass_utils import run_bass_kernel_spmd

    shuffled = [np.asarray(a).reshape(-1, B) for a in (
        L0_conv_dw_w, L0_conv_dw_b, L0_conv_bn2_g, L0_conv_bn2_b, L0_conv_bn2_m, L0_conv_bn2_v,
        L0_conv_bn3_g, L0_conv_bn3_b, L0_conv_bn3_m, L0_conv_bn3_v)]
    plain = [np.asarray(a).reshape(1, B) for a in (
        L0_conv_b1, L0_conv_bn1_g, L0_conv_bn1_b, L0_conv_bn1_m, L0_conv_bn1_v)]
    after = np.concatenate(shuffled)
    after = after.reshape(-1, MID, GROUPS).transpose(0, 2, 1).reshape(-1, B)
    par_mid = np.ascontiguousarray(np.concatenate([after] + plain).T)
    par_out = np.stack([np.asarray(a) for a in (
        L0_conv_b2, L0_conv_bn4_g, L0_conv_bn4_b, L0_conv_bn4_m, L0_conv_bn4_v)])
    arrays = {
        "x": np.ascontiguousarray(np.asarray(x).reshape(N_IMG * H * W, C)),
        "L0_conv_w1": np.ascontiguousarray(L0_conv_w1),
        "L0_conv_w2": np.ascontiguousarray(L0_conv_w2),
        "par_mid": par_mid,
        "par_out": par_out,
    }
    nc = bacc.Bacc("TRN2", target_bir_lowering=False, num_devices=1)
    args = [nc.dram_tensor(name, arrays[name].shape, FP32, kind="ExternalInput").ap() for name in INPUTS]
    out = nc.dram_tensor("out", (N_IMG * H * W, C), FP32, kind="ExternalOutput").ap()
    build(nc, *args, out)
    result = run_bass_kernel_spmd(nc, [arrays], core_ids=[0])
    return result.results[0]["out"].reshape(N_IMG, H, W, C)
```

```python
import concourse.bass as bass
from concourse import mybir
from contextlib import ExitStack

FP32 = mybir.dt.float32
BF16 = mybir.dt.bfloat16
ALU = mybir.AluOpType
ACT = mybir.ActivationFunctionType

P = 128
N_IMG, H, W, C = 32, 56, 56, 512
GROUPS = 8
B = C // 4
KC = C // P
CIN, MID = C // GROUPS, B // GROUPS
EPS = 1e-3

TILES = 7
CHUNK = TILES * P
HALF_ROWS = CHUNK // W // 2
HALF = HALF_ROWS * W
HALVES_PER_IMAGE = H // HALF_ROWS
RING = 7
LOOPS = N_IMG * H * W // CHUNK // RING
LAG = 4
TAP_LAG = 2
FIRST_LOADS = 4
AHEAD = 2
T_BUFS, OUT_BANKS = 2, 3
T_GROUPS = [(0, 1), (2, 3), (4, 5), (6,)]
ACT_SEEDS = [2, 4, 6]
DVE_SEEDS = [t for t in range(TILES) if t not in ACT_SEEDS]

SIDE_TAPS = [(dr, dc) for dc in (-1, 1) for dr in (0, -1, 1)] + [(-1, 0), (1, 0)]

TAP0 = 0
DW_B, G2, B2, M2, V2, G3, B3, M3, V3, C1_B, G1, B1, M1, V1 = range(9, 23)
N_PAR = 23
O_B, O_G4, O_B4, O_M4, O_V4 = range(5)


def tap_column(dr, dc):
    return TAP0 + 3 * (dr + 1) + dc + 1


def row_groups(i):
    groups = []
    for image in range(RING * CHUNK // W // H):
        top, bottom = image * H, (image + 1) * H

        def ready(rows):
            return bottom if rows >= bottom else max(top, rows - 1)

        lo, hi = ready(2 * HALF_ROWS * i), ready(2 * HALF_ROWS * (i + 1))
        if hi > lo:
            groups.append((lo, hi))
    return groups


GROUP_ROWS = [g for i in range(RING) for g in row_groups(i)]
GROUPS_BEFORE = [sum(len(row_groups(j)) for j in range(i)) for i in range(RING + 1)]


def rows_of(x3, lo, hi, dc):
    return x3[:, lo * W:hi * W].rearrange("p (r c) -> p r c", c=W)[:, :, max(0, dc):W + min(0, dc)]


def build(nc, x, w1, w2, par_mid, par_out, out):
    x_c = x.rearrange("(t p) c -> p t c", p=P)
    out_c = out.rearrange("(t p) c -> p t c", p=P)
    ctx = ExitStack()
    with ctx:
        def sb(name, shape):
            return ctx.enter_context(nc.sbuf_tensor(name, shape, FP32))

        def pb(name, banks=1):
            return ctx.enter_context(nc.psum_tensor(name, [P, banks * C], FP32))

        def sem(name):
            return ctx.enter_context(nc.semaphore(name))

        x_sb = sb("x_sb", [P, RING, TILES, C])
        xT = sb("xT", [P, KC, CHUNK])
        r_sb = sb("r_sb", [P, RING * CHUNK])
        s_sb = sb("s_sb", [P, RING * CHUNK])
        w1_sb = sb("w1_sb", [P, KC, 2 * MID])
        w2_sb = sb("w2_sb", [P, C])
        par = sb("par", [P, N_PAR])
        po = sb("po", [P, 5, C])
        bias_sb = sb("bias_sb", [P, C])
        ident = sb("ident", [P, P])
        bias3 = ctx.enter_context(nc.sbuf_tensor("bias3", [P, C], BF16))
        part = ctx.enter_context(nc.sbuf_tensor("part", [P, 3, C], BF16))
        ones = ctx.enter_context(nc.sbuf_tensor("ones", [P, P], BF16))
        beta_b = sb("beta_b", [P, P])
        tmp = sb("tmp", [P, 16])
        newton = sb("newton", [P, C])
        sq_in, sq_out = sb("sq_in", [P, 3 + C]), sb("sq_out", [P, 3 + C])

        t_ps = [pb(f"t_ps{i}", 2) for i in range(T_BUFS)]
        o_ps = [pb(f"o_ps{i}") for i in range(OUT_BANKS)]
        c_ps = pb("c_ps")

        loaded = [sem(f"loaded{i}") for i in range(RING)]
        stored = [sem(f"stored{i}") for i in range(RING)]
        mid_in, w1_in, w2_in, out_in = sem("mid_in"), sem("w1_in"), sem("w2_in"), sem("out_in")
        zeroed = sem("zeroed")
        ident_done = sem("ident_done")
        sqrt_in, sqrt_done = sem("sqrt_in"), sem("sqrt_done")
        prep = sem("prep")
        weights_ready = sem("weights_ready")
        banks_written = sem("banks_written")
        setup_done = sem("setup_done")
        t_done = sem("t_done")
        xt_ready = sem("xt_ready")
        c1_done = sem("c1_done")
        r_ready = sem("r_ready")
        s_begun = sem("s_begun")
        tapped = sem("tapped")
        seeded_dve = sem("seeded_dve")
        seeded_act = sem("seeded_act")
        c2_done = sem("c2_done")
        out_ready = sem("out_ready")

        block = ctx.enter_context(nc.Block())

        def wait(eng, s, count):
            if not (isinstance(count, int) and count <= 0):
                eng.wait_ge(s, count)

        def out_bank(i, t):
            return (TILES * (i % RING) + t) % OUT_BANKS

        def before_in_bank(i, t):
            return next(d for d in range(1, 2 * OUT_BANKS)
                        if out_bank(i + (t - d) // TILES, (t - d) % TILES) == out_bank(i, t))

        def steps(eng, step):
            for i in range(RING):
                step(0, i)
            with eng.Fori(1, LOOPS) as loop:
                for i in range(RING):
                    step(loop, i)
            for i in range(LAG):
                step(LOOPS, i)

        def chunk_exists(loop, i, lag):
            return not isinstance(loop, int) or 0 <= RING * loop + i - lag < RING * LOOPS

        @block.sync
        def _(sp):
            def load(loop, i):
                g = loop * RING + i
                sp.dma_start(x_sb[:, i % RING], x_c[:, bass.ds(g * TILES, TILES), :]).then_inc(loaded[i % RING], 16)

            for i in range(FIRST_LOADS):
                load(0, i)

            def step(loop, i):
                if chunk_exists(loop, i, LAG):
                    g = loop * RING + i - LAG
                    sp.wait_ge(out_ready, (g + 1) * TILES)
                    slot = (i - LAG) % RING
                    sp.dma_start(out_c[:, bass.ds(g * TILES, TILES), :], x_sb[:, slot]).then_inc(stored[slot], 16)
                if chunk_exists(loop, i, -AHEAD) and not (isinstance(loop, int) and RING * loop + i + AHEAD < FIRST_LOADS):
                    ahead = i + AHEAD
                    slot = ahead % RING
                    g = loop * RING + ahead
                    wait(sp, stored[slot], 16 * (loop + ahead // RING))
                    sp.dma_start(x_sb[:, slot], x_c[:, bass.ds(g * TILES, TILES), :]).then_inc(loaded[slot], 16)

            for i in range(RING):
                step(0, i)
            with sp.Fori(1, LOOPS - 1) as loop:
                for i in range(RING):
                    step(loop, i)
            for i in range(RING + LAG):
                step(LOOPS - 1 + i // RING, i % RING)
            for slot in range(RING):
                sp.wait_ge(stored[slot], 16 * LOOPS)

        @block.gpsimd
        def _(pool):
            def place_w2():
                for j in range(MID):
                    pool.dma_start(w2_sb[j:j + MID * (GROUPS - 1) + 1:MID, CIN * (j // 2):CIN * (j // 2 + 1)],
                                   w2[j // 2, GROUPS * (j % 2):GROUPS * (j % 2 + 1), :]).then_inc(w2_in, 16)

            pool.memset(w1_sb[:, :, :], 0.0).then_inc(zeroed, 1)
            pool.memset(w2_sb[:, :], 0.0).then_inc(zeroed, 1)
            pool.memset(ident[:, :], 0.0).then_inc(ident_done, 1)
            pool.wait_ge(ident_done, 1)
            pool.affine_select(out=ident[:, :], in_=ident[:, :], compare_op=ALU.not_equal, fill=1.0, base=0,
                               pattern=[[-1, P]], channel_multiplier=1).then_inc(ident_done, 1)
            pool.wait_ge(zeroed, 2)
            place_w2()

        @block.scalar
        def _(act):
            act.dma_start(par[:, :], par_mid).then_inc(mid_in, 16)
            act.dma_start(po[:, :, :].rearrange("p k c -> p (k c)"),
                          par_out.rearrange("(a k) c -> a (k c)", a=1).broadcast_to([P, 5 * C])).then_inc(out_in, 16)
            act.wait_ge(zeroed, 2)
            w1_g = w1.rearrange("(k e) c m -> e c k m", e=2)
            for e in range(2):
                act.dma_start(w1_sb[e * CIN:(e + 1) * CIN, :, e * MID:(e + 1) * MID], w1_g[e]).then_inc(w1_in, 16)
            act.wait_ge(sqrt_in, 1)
            nc.scalar.activation(sq_out[:, :], sq_in[:, :], ACT.Sqrt).then_inc(sqrt_done, 1)
            act.wait_ge(weights_ready, 1)

            def copy_xt(loop, i, k):
                act.wait_ge(t_done, (loop * RING + i) * len(T_GROUPS) + k + 1)
                tiles = T_GROUPS[k]
                lo, hi = tiles[0] * P, (tiles[-1] + 1) * P
                nc.scalar.copy(xT[:, :, lo:hi].rearrange("p k (t m) -> p t k m", m=P),
                               t_ps[k % T_BUFS][:, 0:len(tiles) * C].rearrange("p (t k m) -> p t k m", k=KC, m=P))\
                    .then_inc(xt_ready, 1)

            def relu_r(loop, i, e):
                act.wait_ge(c1_done, (loop * RING + i) * 2 + e + 1)
                at = ((2 * i + e) % (2 * RING)) * HALF
                nc.scalar.activation(r_sb[:, at:at + HALF], c_ps[:, 0:HALF], ACT.Relu, bias=tmp[:, 15:16],
                                     scale=tmp[:, 14:15]).then_inc(r_ready, 1)

            def centre_tap(loop, i, k):
                act.wait_ge(r_ready, (loop * RING + i) * 2 + 2)
                lo, hi = row_groups(i % RING)[k]
                nc.scalar.activation(s_sb[:, lo * W:hi * W], r_sb[:, lo * W:hi * W], ACT.Copy,
                                     scale=par[:, tap_column(0, 0):tap_column(0, 0) + 1]).then_inc(s_begun, 1)

            def seed(loop, i, t):
                wait(act, out_ready, (loop * RING + i) * TILES + t - before_in_bank(i, t) + 1)
                nc.scalar.copy(o_ps[out_bank(i, t)][:, :], x_sb[:, i % RING, t]).then_inc(seeded_act, 1)

            def relu_out(loop, i, t):
                act.wait_ge(c2_done, (loop * RING + i) * TILES + t + 1)
                nc.scalar.activation(x_sb[:, i % RING, t], o_ps[out_bank(i, t)][:, :], ACT.Relu).then_inc(out_ready, 1)

            def step(loop, i):
                for t in range(TILES):
                    if t % 2 == 0 and chunk_exists(loop, i, 0):
                        copy_xt(loop, i, t // 2)
                    if chunk_exists(loop, i, LAG):
                        if t + 2 in ACT_SEEDS:
                            seed(loop, i - LAG, t + 2)
                        relu_out(loop, i - LAG, t)
                    if t == 0 and chunk_exists(loop, i, 1):
                        relu_r(loop, i - 1, 1)
                    if t in (1, 3) and chunk_exists(loop, i, 1) and t // 2 < len(row_groups((i - 1) % RING)):
                        centre_tap(loop, i - 1, t // 2)
                    if t == 4 and chunk_exists(loop, i, 0):
                        relu_r(loop, i, 0)

            steps(act, step)

        @block.vector
        def _(dve):
            count = [0]

            def then(ins):
                count[0] += 1
                ins.then_inc(prep, 1)
                dve.wait_ge(prep, count[0])

            def col(c):
                return par[:, c:c + 1]

            def tcol(c):
                return tmp[:, c:c + 1]

            dve.wait_ge(mid_in, 16)
            for k, v in enumerate((V1, V2, V3)):
                then(nc.vector.tensor_scalar(sq_in[:, k:k + 1], col(v), EPS, None, ALU.add))
            dve.wait_ge(out_in, 16)
            nc.vector.tensor_scalar(sq_in[:, 3:3 + C], po[:, O_V4, :], EPS, None, ALU.add).then_inc(sqrt_in, 1)
            dve.wait_ge(sqrt_done, 1)
            then(nc.vector.reciprocal(sq_out[:, :], sq_out[:, :]))
            full = [(sq_in[:, 0:3], sq_out[:, 0:3], newton[:, 0:3]), (sq_in[:, 3:3 + C], sq_out[:, 3:3 + C], newton[:, :])]
            for _ in range(2):
                for v, y, n in full:
                    then(nc.vector.tensor_tensor(n, y, y, ALU.mult))
                    then(nc.vector.tensor_tensor(n, n, v, ALU.mult))
                    then(nc.vector.tensor_scalar(n, n, -0.5, 1.5, ALU.mult, ALU.add))
                    then(nc.vector.tensor_tensor(y, y, n, ALU.mult))
            inv1, inv2, inv3, inv4 = sq_out[:, 0:1], sq_out[:, 1:2], sq_out[:, 2:3], sq_out[:, 3:3 + C]
            then(nc.vector.tensor_tensor(tcol(14), col(G1), inv1, ALU.mult))
            then(nc.vector.tensor_tensor(tcol(0), col(C1_B), col(M1), ALU.subtract))
            then(nc.vector.scalar_tensor_tensor(tcol(15), tcol(0), tcol(14), col(B1), ALU.mult, ALU.add))
            then(nc.vector.tensor_tensor(tcol(1), col(G2), inv2, ALU.mult))
            then(nc.vector.tensor_tensor(tcol(2), col(G3), inv3, ALU.mult))
            then(nc.vector.tensor_tensor(tcol(3), tcol(1), tcol(2), ALU.mult))
            then(nc.vector.tensor_tensor(tcol(4), col(DW_B), col(M2), ALU.subtract))
            then(nc.vector.scalar_tensor_tensor(tcol(5), tcol(4), tcol(1), col(B2), ALU.mult, ALU.add))
            then(nc.vector.tensor_tensor(tcol(6), tcol(5), col(M3), ALU.subtract))
            then(nc.vector.scalar_tensor_tensor(tcol(7), tcol(6), tcol(2), col(B3), ALU.mult, ALU.add))
            then(nc.vector.tensor_scalar(par[:, TAP0:TAP0 + 9], par[:, TAP0:TAP0 + 9], tcol(3), None, ALU.mult))
            then(nc.vector.tensor_tensor(newton[:, :], po[:, O_G4, :], inv4, ALU.mult))
            dve.wait_ge(w2_in, 16 * MID)
            then(nc.vector.tensor_tensor(w2_sb[:, :], w2_sb[:, :], newton[:, :], ALU.mult))
            then(nc.vector.tensor_tensor(bias_sb[:, :], po[:, O_B, :], po[:, O_M4, :], ALU.subtract))
            then(nc.vector.tensor_tensor(bias_sb[:, :], bias_sb[:, :], newton[:, :], ALU.mult))
            then(nc.vector.tensor_tensor(bias_sb[:, :], bias_sb[:, :], po[:, O_B4, :], ALU.add))
            then(nc.vector.memset(beta_b[:, :], 1.0))
            then(nc.vector.memset(ones[:, :], 1.0))
            then(nc.vector.memset(bias3[:, :], 0.0))
            nc.vector.tensor_scalar(beta_b[:, :], beta_b[:, :], tcol(7), None, ALU.mult).then_inc(weights_ready, 1)
            dve.wait_ge(banks_written, OUT_BANKS)
            then(nc.vector.tensor_tensor(bias_sb[:, :], bias_sb[:, :], o_ps[0][:, :], ALU.add))
            then(nc.vector.tensor_copy(newton[:, :], bias_sb[:, :]))
            for k in range(3):
                then(nc.vector.tensor_copy(part[:, k], newton[:, :]))
                then(nc.vector.tensor_tensor(newton[:, :], newton[:, :], part[:, k], ALU.subtract))
            for k in range(3):
                nc.vector.tensor_copy(bias3[32 * k:32 * k + 1, :], part[32 * k:32 * k + 1, k]).then_inc(setup_done, 1)

            def seed(loop, i, t):
                before = (loop * RING + i) * TILES + t - before_in_bank(i, t)
                wait(dve, out_ready, before + 1)
                nc.vector.tensor_tensor(o_ps[out_bank(i, t)][:, :], x_sb[:, i % RING, t], bias_sb[:, :],
                                        ALU.add).then_inc(seeded_dve, 1)

            def tap(loop, i, group, k):
                lo, hi = row_groups(i % RING)[group]
                dr, dc = SIDE_TAPS[k]
                n = loop * len(GROUP_ROWS) + GROUPS_BEFORE[i % RING] + (i // RING) * len(GROUP_ROWS) + group
                if k == 0:
                    dve.wait_ge(s_begun, n + 1)
                else:
                    wait_tap(loop, i, group, k)
                a, b = lo, hi
                if dr == -1 and lo % H == 0:
                    a = lo + 1
                if dr == 1 and hi % H == 0:
                    b = hi - 1
                dst = rows_of(s_sb, a, b, -dc)
                nc.vector.scalar_tensor_tensor(dst, rows_of(r_sb, a + dr, b + dr, dc),
                                               par[:, tap_column(dr, dc):tap_column(dr, dc) + 1], dst,
                                               ALU.mult, ALU.add).then_inc(tapped, 1)

            def wait_tap(loop, i, group, k):
                groups = len(row_groups(i % RING))
                done = (loop * len(GROUP_ROWS) + (i // RING) * len(GROUP_ROWS) + GROUPS_BEFORE[i % RING]) * len(SIDE_TAPS)
                dve.wait_ge(tapped, done + (k - 1) * groups + group + 1)

            def step(loop, i):
                work = []
                if chunk_exists(loop, i, TAP_LAG):
                    work = [(group, k) for k in range(len(SIDE_TAPS))
                            for group in range(len(row_groups((i - TAP_LAG) % RING)))]
                for t in range(TILES):
                    if chunk_exists(loop, i, LAG) and t in DVE_SEEDS:
                        seed(loop, i - LAG, t)
                    for group, k in work[t * len(work) // TILES:(t + 1) * len(work) // TILES]:
                        tap(loop, i - TAP_LAG, group, k)

            steps(dve, step)

        @block.tensor
        def _(pe):
            pe.wait_ge(ident_done, 2)

            def write_banks():
                pe.wait_ge(weights_ready, 1)
                for bank in o_ps:
                    nc.tensor.matmul(bank[:, :], beta_b[:, :], w2_sb[:, :], start=True, stop=True).then_inc(banks_written, 1)
                pe.wait_ge(setup_done, 3)

            def transpose_tiles(loop, i, k):
                if k == 0:
                    pe.wait_ge(loaded[i % RING], 16 * (loop + 1))
                wait(pe, xt_ready, (loop * RING + i) * len(T_GROUPS) + k - T_BUFS + 1)
                for m, t in enumerate(T_GROUPS[k]):
                    for b in range(KC):
                        last = nc.tensor.transpose(t_ps[k % T_BUFS][:, (m * KC + b) * P:(m * KC + b + 1) * P],
                                                   x_sb[:, i % RING, t, b * P:(b + 1) * P], ident[:, :])
                last.then_inc(t_done, 1)

            def conv1(loop, i, e):
                if isinstance(loop, int) and loop == 0 and i == 0 and e == 0:
                    pe.wait_ge(w1_in, 32)
                n = (loop * RING + i) * 2 + e
                pe.wait_ge(xt_ready, (loop * RING + i) * len(T_GROUPS) + (len(T_GROUPS) if e else 2))
                wait(pe, r_ready, n)
                for k in range(KC):
                    last = nc.tensor.matmul(c_ps[2 * MID * k:2 * MID * (k + 1), 0:HALF], w1_sb[:, k],
                                            xT[:, k, e * HALF:(e + 1) * HALF], start=True, stop=True)
                last.then_inc(c1_done, 1)

            def conv2(loop, i, t):
                n = loop * RING + i
                if t == 0:
                    j = i % RING
                    last_row = 2 * HALF_ROWS * (j + 1)
                    groups = next(m + 1 for m, (lo, hi) in enumerate(GROUP_ROWS) if hi >= last_row)
                    groups = next(c for c in GROUPS_BEFORE if c >= groups)
                    pe.wait_ge(tapped, ((loop + i // RING) * len(GROUP_ROWS) + groups) * len(SIDE_TAPS))
                at = (i % RING) * CHUNK + t * P
                if t in ACT_SEEDS:
                    pe.wait_ge(seeded_act, n * len(ACT_SEEDS) + ACT_SEEDS.index(t) + 1)
                    nc.tensor.matmul(o_ps[out_bank(i, t)][:, :], ones[:, :], bias3[:, :], start=False, stop=False,
                                     skip_group_check=True)
                else:
                    pe.wait_ge(seeded_dve, n * len(DVE_SEEDS) + DVE_SEEDS.index(t) + 1)
                nc.tensor.matmul(o_ps[out_bank(i, t)][:, :], s_sb[:, at:at + P], w2_sb[:, :], start=False, stop=True,
                                 skip_group_check=True).then_inc(c2_done, 1)

            def step(loop, i):
                if isinstance(loop, int) and loop == 0 and i == 2:
                    write_banks()
                for t in range(TILES):
                    if t % 2 == 0 and chunk_exists(loop, i, 0):
                        transpose_tiles(loop, i, t // 2)
                    if chunk_exists(loop, i, LAG):
                        conv2(loop, i - LAG, t)
                    if t == 0 and chunk_exists(loop, i, 1):
                        conv1(loop, i - 1, 1)
                    if t == 4 and chunk_exists(loop, i, 0):
                        conv1(loop, i, 0)

            steps(pe, step)


INPUTS = ["x", "L0_conv_w1", "L0_conv_w2", "par_mid", "par_out"]


def kernel(x, L0_conv_w1, L0_conv_b1, L0_conv_bn1_g, L0_conv_bn1_b, L0_conv_bn1_m, L0_conv_bn1_v, L0_conv_dw_w,
           L0_conv_dw_b, L0_conv_bn2_g, L0_conv_bn2_b, L0_conv_bn2_m, L0_conv_bn2_v, L0_conv_bn3_g, L0_conv_bn3_b,
           L0_conv_bn3_m, L0_conv_bn3_v, L0_conv_w2, L0_conv_b2, L0_conv_bn4_g, L0_conv_bn4_b, L0_conv_bn4_m,
           L0_conv_bn4_v):
    import numpy as np
    from concourse import bacc
    from concourse.bass_utils import run_bass_kernel_spmd

    shuffled = [np.asarray(a).reshape(-1, B) for a in (
        L0_conv_dw_w, L0_conv_dw_b, L0_conv_bn2_g, L0_conv_bn2_b, L0_conv_bn2_m, L0_conv_bn2_v,
        L0_conv_bn3_g, L0_conv_bn3_b, L0_conv_bn3_m, L0_conv_bn3_v)]
    plain = [np.asarray(a).reshape(1, B) for a in (
        L0_conv_b1, L0_conv_bn1_g, L0_conv_bn1_b, L0_conv_bn1_m, L0_conv_bn1_v)]
    after = np.concatenate(shuffled)
    after = after.reshape(-1, MID, GROUPS).transpose(0, 2, 1).reshape(-1, B)
    par_mid = np.ascontiguousarray(np.concatenate([after] + plain).T)
    par_out = np.stack([np.asarray(a) for a in (
        L0_conv_b2, L0_conv_bn4_g, L0_conv_bn4_b, L0_conv_bn4_m, L0_conv_bn4_v)])
    arrays = {
        "x": np.ascontiguousarray(np.asarray(x).reshape(N_IMG * H * W, C)),
        "L0_conv_w1": np.ascontiguousarray(L0_conv_w1),
        "L0_conv_w2": np.ascontiguousarray(L0_conv_w2),
        "par_mid": par_mid,
        "par_out": par_out,
    }
    nc = bacc.Bacc("TRN2", target_bir_lowering=False, num_devices=1)
    args = [nc.dram_tensor(name, arrays[name].shape, FP32, kind="ExternalInput").ap() for name in INPUTS]
    out = nc.dram_tensor("out", (N_IMG * H * W, C), FP32, kind="ExternalOutput").ap()
    build(nc, *args, out)
    result = run_bass_kernel_spmd(nc, [arrays], core_ids=[0])
    return result.results[0]["out"].reshape(N_IMG, H, W, C)
```

```python
import concourse.bass as bass
from concourse import mybir
from contextlib import ExitStack

FP32 = mybir.dt.float32
BF16 = mybir.dt.bfloat16
ALU = mybir.AluOpType
ACT = mybir.ActivationFunctionType

P = 128
N_IMG, H, W, C = 32, 56, 56, 512
GROUPS = 8
B = C // 4
KC = C // P
CIN, MID = C // GROUPS, B // GROUPS
EPS = 1e-3

TILES = 7
CHUNK = TILES * P
HALF_ROWS = CHUNK // W // 2
HALF = HALF_ROWS * W
RING = 7
LOOPS = N_IMG * H * W // CHUNK // RING
LAG = 4
TAP_LAG = 2
FIRST_LOADS = 4
AHEAD = 2
T_BUFS, OUT_BANKS = 2, 4
FIRST_PARTS = [(0, 1), (1, 2), (2, 3), (3, 5), (5, TILES)]
PARTS = [(0, 4), (4, TILES)]
BIAS_ROWS = [0, 64, 96]
THREE_ACT_SEEDS = [1, 2]
ACT_SEEDS = [[2, 4, 6] if i in THREE_ACT_SEEDS else [2, 5] for i in range(RING)]
TAKEN_OVER = 2

SIDE_TAPS = [(dr, dc) for dc in (-1, 1) for dr in (0, -1, 1)] + [(-1, 0), (1, 0)]
EARLY = len(SIDE_TAPS) // 2
EARLY_TAPS, LATE_TAPS = range(EARLY), range(EARLY, len(SIDE_TAPS))

TAP0 = 0
DW_B, G2, B2, M2, G3, B3, M3, C1_B, G1, B1, M1 = range(9, 20)
V1, V2, V3, V4 = range(20, 24)
O_B, O_G4, O_B4, O_M4 = (V4 + KC * k for k in range(1, 5))
N_PAR = V4 + KC * 5
CONST_COLUMNS = P + KC * 2 * MID + N_PAR
N_VAR = 3 + KC


def tap_column(dr, dc):
    return TAP0 + 3 * (dr + 1) + dc + 1


def rows_ready(i):
    return max(0, 2 * HALF_ROWS * i - 1), 2 * HALF_ROWS * (i + 1) - (i < RING - 1)


def tap_pieces(i, k):
    (lo, hi), (dr, dc) = rows_ready(i), SIDE_TAPS[k]
    if dr == 0:
        return [(lo, hi)]
    return [(max(lo, top - min(0, dr)), min(hi, top + H - max(0, dr)))
            for top in range(lo // H * H, hi, H)]


def pieces(chunks, taps):
    return sum(len(tap_pieces(i, k)) for i in chunks for k in taps)


def rows_of(x3, lo, hi, dc):
    return x3[:, lo * W:hi * W].rearrange("p (r c) -> p r c", c=W)[:, :, max(0, dc):W + min(0, dc)]


def build(nc, x, consts, w2, out):
    x_c = x.rearrange("(t p) c -> p t c", p=P)
    out_c = out.rearrange("(t p) c -> p t c", p=P)
    ctx = ExitStack()
    with ctx:
        def sb(name, shape):
            return ctx.enter_context(nc.sbuf_tensor(name, shape, FP32))

        def sem(name):
            return ctx.enter_context(nc.semaphore(name))

        x_sb = sb("x_sb", [P, RING, TILES, C])
        xT = sb("xT", [P, 2, KC, CHUNK])
        r_sb = sb("r_sb", [P, RING * CHUNK])
        s_sb = sb("s_sb", [P, RING * CHUNK])
        const_sb = sb("const_sb", [P, CONST_COLUMNS])
        ident = const_sb[:, 0:P]
        w1_sb = const_sb[:, P:P + KC * 2 * MID].rearrange("p (k m) -> p k m", k=KC)
        par = const_sb[:, P + KC * 2 * MID:CONST_COLUMNS]
        w2_sb = sb("w2_sb", [P, C])
        bias_sb = sb("bias_sb", [P, C])
        bias3 = ctx.enter_context(nc.sbuf_tensor("bias3", [P, C], BF16))
        ones3 = ctx.enter_context(nc.sbuf_tensor("ones3", [P, P], BF16))
        zeros = ctx.enter_context(nc.sbuf_tensor("zeros", [1, C], BF16))
        beta_b = sb("beta_b", [P, P])
        ones_f = sb("ones_f", [P, P])
        spread = sb("spread", [P, 2 * KC, P])
        work_sb = sb("work_sb", [P, 9 + 2 * KC])
        scale1, bias1, scale2, scale3, scale23, c1_centred, dw_centred, after_bn2, beta = (
            work_sb[:, k:k + 1] for k in range(9))
        scale4, offset4 = work_sb[:, 9:9 + KC], work_sb[:, 9 + KC:9 + 2 * KC]
        newton = sb("newton", [P, N_VAR])
        sq_in, sq_out = sb("sq_in", [P, N_VAR]), sb("sq_out", [P, N_VAR])
        rest = sb("rest", [P, C])

        ps = ctx.enter_context(nc.psum_tensor("ps", [P, 8, C], FP32))
        t_ps = [ps[:, k] for k in range(T_BUFS)]
        c_ps = [ps[:, T_BUFS + e, 0:HALF] for e in range(2)]
        o_ps = [ps[:, T_BUFS + 2 + k] for k in range(OUT_BANKS)]

        loaded = [[sem(f"loaded{i}_{p}") for p in range(len(PARTS))] for i in range(RING)]
        first_loaded = [sem(f"first_loaded{k}") for k in range(len(FIRST_PARTS))]
        last_stored = [sem(f"last_stored{t}") for t in range(TILES)]
        stored = [[sem(f"stored{i}_{p}") for p in range(len(PARTS))] for i in range(RING)]
        consts_in, w2_in = sem("consts_in"), sem("w2_in")
        filled = sem("filled")
        sqrt_in, sqrt_done = sem("sqrt_in"), sem("sqrt_done")
        prep = sem("prep")
        taps_ready = sem("taps_ready")
        bn1_ready = sem("bn1_ready")
        spread_ready = sem("spread_ready")
        scale_ready = sem("scale_ready")
        bias_copied = sem("bias_copied")
        split = sem("split")
        weights_ready = sem("weights_ready")
        banks_written = sem("banks_written")
        t_done = sem("t_done")
        xt_ready = sem("xt_ready")
        c1_done = sem("c1_done")
        r_ready = sem("r_ready")
        s_begun = sem("s_begun")
        tapped_early = sem("tapped_early")
        tapped_late = sem("tapped_late")
        seeded_dve = sem("seeded_dve")
        seeded_act = sem("seeded_act")
        c2_done = sem("c2_done")
        out_ready = sem("out_ready")

        block = ctx.enter_context(nc.Block())

        def seeded_by(engine, loop, i):
            by_act = ACT_SEEDS[i % RING]
            if isinstance(loop, int) and loop == LOOPS and i < TAKEN_OVER - LAG:
                by_act = range(i == -LAG, TILES)
            return [t for t in range(TILES) if (t in by_act) == (engine == "scalar")]

        def seeds_until(engine, loop, i, t):
            def of_chunks(loop, chunks):
                return sum(len(seeded_by(engine, loop, j)) for j in chunks)

            in_chunk = len([u for u in seeded_by(engine, loop, i) if u <= t])
            if isinstance(loop, int) and loop == LOOPS:
                return (LOOPS - 1) * of_chunks(0, range(RING)) + of_chunks(0, range(RING - LAG)) \
                    + of_chunks(LOOPS, range(-LAG, i)) + in_chunk
            return (loop + i // RING) * of_chunks(0, range(RING)) + of_chunks(0, range(i % RING)) + in_chunk

        def wait(eng, s, count):
            if not (isinstance(count, int) and count <= 0):
                eng.wait_ge(s, count)

        def t_buffer(i, t):
            return (TILES * (i % RING) + t) % T_BUFS

        def transposes_first(loop, i):
            return i % RING != 0 and not (isinstance(loop, int) and (loop, i) == (0, 1))

        def out_bank(t):
            return t % OUT_BANKS

        def before_in_bank(t):
            return next(d for d in range(1, 2 * OUT_BANKS) if out_bank((t - d) % TILES) == out_bank(t))

        def steps(eng, step):
            for i in range(RING):
                step(0, i)
            with eng.Fori(1, LOOPS) as loop:
                for i in range(RING):
                    step(loop, i)
            for i in range(LAG):
                step(LOOPS, i)

        def chunk_exists(loop, i, lag):
            return not isinstance(loop, int) or 0 <= RING * loop + i - lag < RING * LOOPS

        @block.sync
        def _(sp):
            sp.dma_start(const_sb[:, :], consts).then_inc(consts_in, 16)
            for k, (lo, hi) in enumerate(FIRST_PARTS):
                sp.dma_start(x_sb[:, 0, lo:hi], x_c[:, lo:hi, :]).then_inc(first_loaded[k], 16)

            def load(loop, i, part):
                slot = i % RING
                lo, hi = PARTS[part]
                for p in range(len(PARTS)):
                    wait(sp, stored[slot][p], 16 * (loop + i // RING))
                sp.dma_start(x_sb[:, slot, lo:hi], x_c[:, bass.ds((loop * RING + i) * TILES + lo, hi - lo), :])\
                    .then_inc(loaded[slot][part], 16)

            def store(loop, i, part):
                slot = i % RING
                lo, hi = PARTS[part]
                first = (loop * RING + i) * TILES
                sp.wait_ge(out_ready, first + hi)
                sp.dma_start(out_c[:, bass.ds(first + lo, hi - lo), :], x_sb[:, slot, lo:hi])\
                    .then_inc(stored[slot][part], 16)

            load(0, 1, 0)
            sp.dma_start(w2_sb[:, :], w2).then_inc(w2_in, 16)
            load(0, 1, 1)
            for i in range(2, FIRST_LOADS):
                for part in range(len(PARTS)):
                    load(0, i, part)

            def step(loop, i):
                for part in range(len(PARTS)):
                    if chunk_exists(loop, i, LAG):
                        store(loop, i - LAG, part)
                    if chunk_exists(loop, i, -AHEAD) and not (isinstance(loop, int) and RING * loop + i + AHEAD < FIRST_LOADS):
                        load(loop, i + AHEAD, part)

            for i in range(RING):
                step(0, i)
            with sp.Fori(1, LOOPS - 1) as loop:
                for i in range(RING):
                    step(loop, i)
            for i in range(RING + LAG - 1):
                step(LOOPS - 1 + i // RING, i % RING)
            for t in range(TILES):
                n = (LOOPS * RING - 1) * TILES + t
                sp.wait_ge(out_ready, n + 1)
                sp.dma_start(out_c[:, n:n + 1, :], x_sb[:, RING - 1, t:t + 1]).then_inc(last_stored[t], 16)
            for slot in range(RING):
                for s in stored[slot]:
                    sp.wait_ge(s, 16 * (LOOPS - (slot == RING - 1)))
            for t in range(TILES):
                sp.wait_ge(last_stored[t], 16)

        @block.gpsimd
        def _(pool):
            pool.memset(ones_f[:, :], 1.0).then_inc(filled, 1)
            pool.memset(zeros[:, :], 0.0).then_inc(filled, 1)
            pool.memset(ones3[:, :], 0.0).then_inc(filled, 1)
            pool.wait_ge(filled, 3)
            for row in BIAS_ROWS:
                pool.memset(ones3[row:row + 1, :], 1.0).then_inc(filled, 1)
            pool.wait_ge(bias_copied, 1)
            nc.gpsimd.tensor_copy(bias3[:, :], bias_sb[:, :]).then_inc(split, 1)
            for k, row in enumerate(BIAS_ROWS[1:]):
                pool.wait_ge(split, 2 * k + 1)
                left = bias_sb if k == 0 else rest
                nc.gpsimd.tensor_tensor(rest[row:P, :], left[row:P, :], bias3[row:P, :], ALU.subtract).then_inc(split, 1)
                pool.wait_ge(split, 2 * k + 2)
                nc.gpsimd.tensor_copy(bias3[row:P, :], rest[row:P, :]).then_inc(split, 1)

        @block.scalar
        def _(act):
            act.wait_ge(sqrt_in, 1)
            nc.scalar.activation(sq_out[:, :], sq_in[:, :], ACT.Sqrt).then_inc(sqrt_done, 1)

            def copy_xt(loop, i, t):
                n = (loop * RING + i) * TILES + t
                act.wait_ge(t_done, n + 1)
                nc.scalar.copy(xT[:, i % RING % 2, :, t * P:(t + 1) * P],
                               t_ps[t_buffer(i, t)].rearrange("p (k m) -> p k m", m=P)).then_inc(xt_ready, 1)

            def relu_r(loop, i, e):
                if isinstance(loop, int) and loop == 0 and i == 0 and e == 0:
                    act.wait_ge(bn1_ready, 1)
                act.wait_ge(c1_done, (loop * RING + i) * 2 + e + 1)
                at = ((2 * i + e) % (2 * RING)) * HALF
                nc.scalar.activation(r_sb[:, at:at + HALF], c_ps[e], ACT.Relu, bias=bias1,
                                     scale=scale1).then_inc(r_ready, 1)

            def centre_tap(loop, i):
                if isinstance(loop, int) and loop == 0 and i == 0:
                    act.wait_ge(taps_ready, 1)
                act.wait_ge(r_ready, (loop * RING + i + 1) * 2)
                lo, hi = rows_ready(i % RING)
                nc.scalar.activation(s_sb[:, lo * W:hi * W], r_sb[:, lo * W:hi * W], ACT.Copy,
                                     scale=par[:, tap_column(0, 0):tap_column(0, 0) + 1]).then_inc(s_begun, 1)

            def seed(loop, i, t):
                wait(act, out_ready, (loop * RING + i) * TILES + t - before_in_bank(t) + 1)
                nc.scalar.copy(o_ps[out_bank(t)], x_sb[:, i % RING, t]).then_inc(seeded_act, 1)

            def seed_if_ours(loop, i, t):
                i, t = i + t // TILES, t % TILES
                if not (isinstance(loop, int) and loop == LOOPS and i == 0) and t in seeded_by("scalar", loop, i):
                    seed(loop, i, t)

            def relu_out(loop, i, t):
                act.wait_ge(c2_done, (loop * RING + i) * TILES + t + 1)
                nc.scalar.activation(x_sb[:, i % RING, t], o_ps[out_bank(t)], ACT.Relu).then_inc(out_ready, 1)

            def step(loop, i):
                for t in range(TILES):
                    if t == 0 and transposes_first(loop, i) and chunk_exists(loop, i, 0):
                        copy_xt(loop, i, t)
                    if t == 0 and chunk_exists(loop, i, 1):
                        for e in range(2):
                            relu_r(loop, i - 1, e)
                        if isinstance(loop, int) and RING * loop + i < LAG:
                            centre_tap(loop, i - 1)
                    if not (t == 0 and transposes_first(loop, i)) and chunk_exists(loop, i, 0):
                        copy_xt(loop, i, t)
                    if chunk_exists(loop, i, LAG):
                        if isinstance(loop, int) and (loop, i, t) == (LOOPS, 0, 0):
                            seed(loop, i - LAG, 1)
                        seed_if_ours(loop, i - LAG, t + 2)
                        relu_out(loop, i - LAG, t)
                    if t == 1 and chunk_exists(loop, i, 1) and not (isinstance(loop, int) and RING * loop + i < LAG):
                        centre_tap(loop, i - 1)

            steps(act, step)

        @block.vector
        def _(dve):
            count = [0]

            def then(ins, steps=1):
                count[0] += steps
                ins.then_inc(prep, 1)
                dve.wait_ge(prep, count[0])

            def col(c):
                return par[:, c:c + 1]

            dve.wait_ge(consts_in, 16)
            nc.vector.tensor_scalar(sq_in[:, :], par[:, V1:V1 + N_VAR], EPS, None, ALU.add).then_inc(sqrt_in, 1)
            then(nc.vector.memset(beta_b[:, :], 1.0))
            dve.wait_ge(sqrt_done, 1)
            v, y, n = sq_in[:, :], sq_out[:, :], newton[:, :]
            then(nc.vector.reciprocal(y, y))
            for _ in range(2):
                then(nc.vector.tensor_tensor(n, y, y, ALU.mult))
                then(nc.vector.tensor_tensor(n, n, v, ALU.mult))
                then(nc.vector.tensor_scalar(n, n, -0.5, 1.5, ALU.mult, ALU.add))
                then(nc.vector.tensor_tensor(y, y, n, ALU.mult))
            inv1, inv2, inv3, inv4 = sq_out[:, 0:1], sq_out[:, 1:2], sq_out[:, 2:3], sq_out[:, 3:3 + KC]
            then(nc.vector.tensor_tensor(scale4, par[:, O_G4:O_G4 + KC], inv4, ALU.mult))
            for k in range(KC):
                nc.vector.tensor_scalar(spread[:, k], ident, scale4[:, k:k + 1], None, ALU.mult)\
                    .then_inc(spread_ready, 1)
            nc.vector.tensor_tensor(c1_centred, col(C1_B), col(M1), ALU.subtract).then_inc(prep, 1)
            then(nc.vector.tensor_tensor(scale1, col(G1), inv1, ALU.mult), 2)
            nc.vector.scalar_tensor_tensor(bias1, c1_centred, scale1, col(B1), ALU.mult, ALU.add).then_inc(bn1_ready, 1)
            nc.vector.tensor_tensor(scale2, col(G2), inv2, ALU.mult).then_inc(prep, 1)
            nc.vector.tensor_tensor(dw_centred, col(DW_B), col(M2), ALU.subtract).then_inc(prep, 1)
            then(nc.vector.tensor_tensor(scale3, col(G3), inv3, ALU.mult), 3)
            nc.vector.tensor_tensor(scale23, scale2, scale3, ALU.mult).then_inc(prep, 1)
            then(nc.vector.scalar_tensor_tensor(after_bn2, dw_centred, scale2, col(B2), ALU.mult, ALU.add), 2)
            nc.vector.tensor_scalar(par[:, TAP0:TAP0 + 9], par[:, TAP0:TAP0 + 9], scale23, None, ALU.mult)\
                .then_inc(taps_ready, 1)
            then(nc.vector.tensor_tensor(after_bn2, after_bn2, col(M3), ALU.subtract))
            then(nc.vector.scalar_tensor_tensor(beta, after_bn2, scale3, col(B3), ALU.mult, ALU.add))
            nc.vector.tensor_scalar(beta_b[:, :], beta_b[:, :], beta, None, ALU.mult).then_inc(weights_ready, 1)
            dve.wait_ge(w2_in, 16)
            dve.wait_ge(scale_ready, 1)
            nc.vector.tensor_tensor(w2_sb[:, :], w2_sb[:, :], o_ps[0], ALU.mult).then_inc(weights_ready, 1)
            then(nc.vector.tensor_tensor(offset4, par[:, O_B:O_B + KC], par[:, O_M4:O_M4 + KC], ALU.subtract))
            then(nc.vector.tensor_tensor(offset4, offset4, scale4, ALU.mult))
            then(nc.vector.tensor_tensor(offset4, offset4, par[:, O_B4:O_B4 + KC], ALU.add))
            for k in range(KC):
                nc.vector.tensor_scalar(spread[:, KC + k], ident, offset4[:, k:k + 1], None, ALU.mult)\
                    .then_inc(spread_ready, 1)

            def finish_bias():
                dve.wait_ge(banks_written, OUT_BANKS)
                nc.vector.tensor_copy(bias_sb[:, :], o_ps[0]).then_inc(bias_copied, 1)

            def seed_if_ours(loop, i, t):
                i, t = i + t // TILES, t % TILES
                exists = not isinstance(loop, int) or 0 <= loop * RING + i < LOOPS * RING
                if exists and t in seeded_by("vector", loop, i):
                    seed(loop, i, t)

            def seed(loop, i, t):
                before = (loop * RING + i) * TILES + t - before_in_bank(t)
                if isinstance(loop, int) and loop == 0 and i == 0 and t == 0:
                    dve.wait_ge(bias_copied, 1)
                wait(dve, out_ready, before + 1)
                nc.vector.tensor_tensor(o_ps[out_bank(t)], x_sb[:, i % RING, t], bias_sb[:, :],
                                        ALU.add).then_inc(seeded_dve, 1)

            def tap(loop, i, k, piece):
                a, b = tap_pieces(i % RING, k)[piece]
                dr, dc = SIDE_TAPS[k]
                if k == 0:
                    dve.wait_ge(s_begun, loop * RING + i + 1)
                else:
                    of_kind = EARLY_TAPS if k - 1 < EARLY else LATE_TAPS
                    before = pieces([i % RING], range(of_kind[0], k))
                    if len(tap_pieces(i % RING, k - 1)) == len(tap_pieces(i % RING, k)):
                        before = pieces([i % RING], range(of_kind[0], k - 1)) + piece + 1
                    dve.wait_ge(tapped_early if k - 1 < EARLY else tapped_late,
                                (loop + i // RING) * pieces(range(RING), of_kind)
                                + pieces(range(i % RING), of_kind) + before)
                dst = rows_of(s_sb, a, b, -dc)
                nc.vector.scalar_tensor_tensor(dst, rows_of(r_sb, a + dr, b + dr, dc),
                                               par[:, tap_column(dr, dc):tap_column(dr, dc) + 1], dst,
                                               ALU.mult, ALU.add).then_inc(tapped_early if k < EARLY else tapped_late, 1)

            def step(loop, i):
                work = []
                for n in range(EARLY):
                    for lag, taps in (TAP_LAG + 1, LATE_TAPS), (TAP_LAG, EARLY_TAPS):
                        if chunk_exists(loop, i, lag) and n < len(taps):
                            work += [(lag, taps[n], piece) for piece in range(len(tap_pieces((i - lag) % RING, taps[n])))]
                for t in range(TILES):
                    for n in range(t * len(work) // TILES, (t + 1) * len(work) // TILES):
                        lag, k, piece = work[n]
                        tap(loop, i - lag, k, piece)
                        if isinstance(loop, int) and loop == 0 and i == TAP_LAG + 1 and k == 0:
                            finish_bias()
                    seed_if_ours(loop, i - LAG, t + 1)

            steps(dve, step)

        @block.tensor
        def _(pe):
            pe.wait_ge(consts_in, 16)

            def spread_scale():
                pe.wait_ge(filled, 6)
                for k in range(KC):
                    pe.wait_ge(spread_ready, k + 1)
                    last = nc.tensor.matmul(o_ps[0][:, k * P:(k + 1) * P], ones_f[:, :], spread[:, k], start=True,
                                            stop=True)
                last.then_inc(scale_ready, 1)

            def write_banks():
                pe.wait_ge(weights_ready, 2)
                nc.tensor.matmul(o_ps[0], beta_b[:, :], w2_sb[:, :], start=True, stop=False, skip_group_check=True)
                for k in range(KC):
                    pe.wait_ge(spread_ready, KC + k + 1)
                    last = nc.tensor.matmul(o_ps[0][:, k * P:(k + 1) * P], ones_f[:, :], spread[:, KC + k],
                                            start=False, stop=True, skip_group_check=True)
                last.then_inc(banks_written, 1)
                for bank in o_ps[1:]:
                    nc.tensor.matmul(bank, ones3[0:1, :], zeros[:, :], start=True, stop=True).then_inc(banks_written, 1)

            def transpose_tile(loop, i, t):
                if isinstance(loop, int) and loop == 0 and i == 0:
                    if t in [lo for lo, hi in FIRST_PARTS]:
                        pe.wait_ge(first_loaded[[lo for lo, hi in FIRST_PARTS].index(t)], 16)
                elif t in [lo for lo, hi in PARTS]:
                    part = [lo for lo, hi in PARTS].index(t)
                    pe.wait_ge(loaded[i % RING][part], 16 * (loop + 1 - (i % RING == 0)))
                wait(pe, xt_ready, (loop * RING + i) * TILES + t - T_BUFS + 1)
                for b in range(KC):
                    last = nc.tensor.transpose(t_ps[t_buffer(i, t)][:, b * P:(b + 1) * P],
                                               x_sb[:, i % RING, t, b * P:(b + 1) * P], ident)
                last.then_inc(t_done, 1)

            def conv1(loop, i):
                n = loop * RING + i
                pe.wait_ge(xt_ready, (n + 1) * TILES)
                wait(pe, r_ready, 2 * n)
                for e in range(2):
                    for k in range(KC):
                        last = nc.tensor.matmul(c_ps[e][2 * MID * k:2 * MID * (k + 1)], w1_sb[:, k],
                                                xT[:, i % RING % 2, k, e * HALF:(e + 1) * HALF], start=True, stop=True)
                    last.then_inc(c1_done, 1)

            def conv2(loop, i, t):
                n = loop * RING + i
                j = i % RING
                if t in (0, TILES - 1):
                    chunks = range(min(RING, j + 1 + (t == TILES - 1)))
                    pe.wait_ge(tapped_late, (loop + i // RING) * pieces(range(RING), LATE_TAPS) + pieces(chunks, LATE_TAPS))
                at = (i % RING) * CHUNK + t * P
                if t in seeded_by("vector", loop, i):
                    pe.wait_ge(seeded_dve, seeds_until("vector", loop, i, t))
                else:
                    pe.wait_ge(seeded_act, seeds_until("scalar", loop, i, t))
                    if isinstance(loop, int) and loop == 0 and i == 0 and t == ACT_SEEDS[0][0]:
                        pe.wait_ge(split, 5)
                    nc.tensor.matmul(o_ps[out_bank(t)], ones3[:, :], bias3[:, :], start=False, stop=False,
                                     skip_group_check=True)
                nc.tensor.matmul(o_ps[out_bank(t)], s_sb[:, at:at + P], w2_sb[:, :], start=False, stop=True,
                                 skip_group_check=True).then_inc(c2_done, 1)

            def step(loop, i):
                for t in range(TILES):
                    if t == 0 and transposes_first(loop, i) and chunk_exists(loop, i, 0):
                        transpose_tile(loop, i, t)
                    if t == 0 and chunk_exists(loop, i, 1):
                        conv1(loop, i - 1)
                        if isinstance(loop, int) and loop == 0 and i == 2:
                            write_banks()
                    if not (t == 0 and transposes_first(loop, i)) and chunk_exists(loop, i, 0):
                        transpose_tile(loop, i, t)
                    if chunk_exists(loop, i, LAG):
                        conv2(loop, i - LAG, t)
                    if isinstance(loop, int) and loop == 0 and i == 0 and t == TILES - 1:
                        spread_scale()

            steps(pe, step)


INPUTS = ["x", "consts", "L0_conv_w2"]


def kernel(x, L0_conv_w1, L0_conv_b1, L0_conv_bn1_g, L0_conv_bn1_b, L0_conv_bn1_m, L0_conv_bn1_v, L0_conv_dw_w,
           L0_conv_dw_b, L0_conv_bn2_g, L0_conv_bn2_b, L0_conv_bn2_m, L0_conv_bn2_v, L0_conv_bn3_g, L0_conv_bn3_b,
           L0_conv_bn3_m, L0_conv_bn3_v, L0_conv_w2, L0_conv_b2, L0_conv_bn4_g, L0_conv_bn4_b, L0_conv_bn4_m,
           L0_conv_bn4_v):
    import numpy as np
    from concourse import bacc
    from concourse.bass_utils import run_bass_kernel_spmd

    shuffled = [np.asarray(a).reshape(-1, B) for a in (
        L0_conv_dw_w, L0_conv_dw_b, L0_conv_bn2_g, L0_conv_bn2_b, L0_conv_bn2_m, L0_conv_bn2_v,
        L0_conv_bn3_g, L0_conv_bn3_b, L0_conv_bn3_m, L0_conv_bn3_v)]
    plain = [np.asarray(a).reshape(1, B) for a in (
        L0_conv_b1, L0_conv_bn1_g, L0_conv_bn1_b, L0_conv_bn1_m, L0_conv_bn1_v)]
    after = np.concatenate(shuffled)
    after = after.reshape(-1, MID, GROUPS).transpose(0, 2, 1).reshape(-1, B)
    taps_to_m2, v2, g3_to_m3, v3 = after[:13], after[13:14], after[14:17], after[17:18]
    outer = [np.asarray(a).reshape(KC, P) for a in (
        L0_conv_bn4_v, L0_conv_b2, L0_conv_bn4_g, L0_conv_bn4_b, L0_conv_bn4_m)]
    params = np.concatenate([taps_to_m2, g3_to_m3] + plain[:4] + [plain[4], v2, v3] + outer).T
    w1 = np.zeros((P, KC, 2 * MID), np.float32)
    for e in range(2):
        w1[e * CIN:(e + 1) * CIN, :, e * MID:(e + 1) * MID] = np.asarray(L0_conv_w1)[e::2].transpose(1, 0, 2)
    w2 = np.zeros((P, C), np.float32)
    for j in range(MID):
        w2[j::MID, CIN * (j // 2):CIN * (j // 2 + 1)] = \
            np.asarray(L0_conv_w2)[j // 2, GROUPS * (j % 2):GROUPS * (j % 2 + 1)]
    arrays = {
        "x": np.ascontiguousarray(np.asarray(x).reshape(N_IMG * H * W, C)),
        "consts": np.ascontiguousarray(np.concatenate([np.eye(P, dtype=np.float32), w1.reshape(P, -1), params], axis=1)),
        "L0_conv_w2": w2,
    }
    nc = bacc.Bacc("TRN2", target_bir_lowering=False, num_devices=1)
    args = [nc.dram_tensor(name, arrays[name].shape, FP32, kind="ExternalInput").ap() for name in INPUTS]
    out = nc.dram_tensor("out", (N_IMG * H * W, C), FP32, kind="ExternalOutput").ap()
    build(nc, *args, out)
    result = run_bass_kernel_spmd(nc, [arrays], core_ids=[0])
    return result.results[0]["out"].reshape(N_IMG, H, W, C)
```
